# Optimizing a Trainium2 kernel written in Bass

```python
import numpy as np
import jax
import jax.numpy as jnp

def _softmax(x, axis=-1):
    return jax.nn.softmax(x, axis=axis)

def _gelu(x):
    return jax.nn.gelu(x, approximate=True)

def _silu(x):
    return jax.nn.silu(x)

def _sigmoid(x):
    return jax.nn.sigmoid(x)

def _layernorm(x, axis=-1, eps=1e-05):
    m = jnp.mean(x, axis=axis, keepdims=True)
    v = jnp.var(x, axis=axis, keepdims=True)
    return (x - m) / jnp.sqrt(v + eps)

def _scatter_add(tgt, idx, src, axis=0):
    return tgt.at[idx].add(src)

def _segment_sum(src, seg, n):
    return jax.ops.segment_sum(src, seg, n)
kernel_name = 'mk_adj_resnorm_d1_adj_r2_efff45'

def setup_inputs(seed: int=0):
    np.random.seed(seed)
    _w = jnp.asarray

    def _rec_inputs():
        import jax
        import jax.numpy as jnp
        _gk = jax.random.key(seed)
        x = -0.000929 + 1 * jax.random.normal(jax.random.fold_in(_gk, 1), (8192, 64), jnp.float32)
        _w = (1.0 + jnp.arange(8192, dtype=jnp.float32)) ** (-0.5)
        _w = _w / _w.mean()
        _pij = jnp.clip(0.000488281 * _w[:, None] * _w[None, :], 0.0, 1.0)
        _a = jax.random.uniform(jax.random.fold_in(_gk, 2), (8192, 8192)) < _pij
        _af = _a.astype(jnp.float32)
        adj = _af
        return (x, adj)
    x, adj = _rec_inputs()

    def _L0_gnn_setup():
        import jax, jax.numpy as jnp
        import numpy as np
        N, D_IN, D_OUT = (8192, 64, 64)
        AVG_DEG = 32.0
        L2_EPS = 1e-12
        key = jax.random.key(seed)
        kx, ka, kw, kb = jax.random.split(key, 4)
        X = jax.random.normal(kx, (N, D_IN), dtype=jnp.float32)
        adj = (jax.random.uniform(ka, (N, N)) < AVG_DEG / N).astype(jnp.float32)
        bound = 1.0 / np.sqrt(2 * D_IN)
        W = jax.random.uniform(kw, (2 * D_IN, D_OUT), dtype=jnp.float32, minval=-bound, maxval=bound)
        b = jax.random.uniform(kb, (D_OUT,), dtype=jnp.float32, minval=-bound, maxval=bound)
        return {'X': X, 'adj': adj, 'W': W, 'b': b}
    _L0_gnn_all = _L0_gnn_setup()
    _L0_gnn_in = {k: v for k, v in _L0_gnn_all.items() if k in ('W', 'b')}
    del _L0_gnn_all
    return {'x': x, 'adj': adj, 'L0_gnn_W': _L0_gnn_in['W'], 'L0_gnn_b': _L0_gnn_in['b']}

def reference(x, adj, L0_gnn_W, L0_gnn_b):
    import jax
    import jax.numpy as jnp

    def _L0_gnn_ref(X, adj, W, b):
        import jax, jax.numpy as jnp
        import numpy as np
        N, D_IN, D_OUT = (8192, 64, 64)
        AVG_DEG = 32.0
        L2_EPS = 1e-12
        deg = jnp.clip(jnp.sum(adj, axis=1, keepdims=True) + 1.0, 1.0, None)
        h_neigh = (adj @ X + X) / deg
        concat = jnp.concatenate([X, h_neigh], axis=1)
        z = concat @ W + b
        out = jax.nn.relu(z)
        norm = jnp.linalg.norm(out, axis=1, keepdims=True)
        return out / jnp.maximum(norm, L2_EPS)
    x = _layernorm(x + _L0_gnn_ref(x, adj, L0_gnn_W, L0_gnn_b), axis=-1)
    return x

_drawn_inputs = setup_inputs


def setup_inputs(seed=0):
    import zlib

    import numpy as np

    out = dict(_drawn_inputs(seed))
    spreads = {}
    factors = {'L0_gnn_b': 3.586}
    for name, (base, spread) in spreads.items():
        noise = np.random.default_rng([zlib.crc32(name.encode()), seed]).standard_normal(out[name].shape)
        drawn = base * np.exp(spread * noise) if base else spread * noise
        out[name] = jnp.asarray(drawn.astype(out[name].dtype))
    for name, factor in factors.items():
        out[name] = (out[name] * factor).astype(out[name].dtype)
    return out
```

```python
from contextlib import ExitStack

import numpy as np

import concourse.bass as bass
from concourse import mybir

N = 8192
D = 64
P = 128
NB = N // P
GB = 8
G = NB // GB
GC = GB * P
HALF = GC // 2
HB = GB // 2
JB = 4
CHUNKS = NB // JB
SLOTS = 8
PASSES = CHUNKS // SLOTS
XPARTS = 4
L2_EPS = 1e-12
LN_EPS = 1e-5

F32 = mybir.dt.float32
ALU = mybir.AluOpType
ACT = mybir.ActivationFunctionType
AX_X = mybir.AxisListType.X


def gnn_resnorm(nc: bass.Bass, x, adj_chunks, w, b, ident, out):
    x_nodes = x.rearrange("(p b) d -> p b d", b=NB)
    out_nodes = out.rearrange("(p b) d -> p b d", b=NB)

    with ExitStack() as ctx:
        def sb(name, shape):
            return ctx.enter_context(nc.sbuf_tensor(name, shape, F32))

        def ps(name, shape):
            return ctx.enter_context(nc.psum_tensor(name, shape, F32))

        def sem(name):
            return ctx.enter_context(nc.semaphore(name))

        ring = sb("ring", [P, SLOTS, JB * GC])
        x_sb = sb("x_sb", [P, NB, D])
        identity = sb("identity", [P, P])
        w_self = sb("w_self", [P, D])
        w_neigh = sb("w_neigh", [P, D])
        bias_row = sb("bias_row", [P, HB, D])
        ones = sb("ones", [P, P])
        ln_eps = sb("ln_eps", [P, 1])
        part_deg = sb("part_deg", [P, JB * GC])
        x_group = sb("x_group", [P, GB, D])
        xT = sb("xT", [P, HALF])
        hT = sb("hT", [P, HALF])
        deg = sb("deg", [P, GB])
        inv_deg = sb("inv_deg", [P, GB])
        z = sb("z", [P, GB, D])
        relu = sb("relu", [P, GB, D])
        square = sb("square", [P, GB, D])
        norm_sq = sb("norm_sq", [P, GB])
        norm = sb("norm", [P, GB])
        inv_norm = sb("inv_norm", [P, GB])
        y = sb("y", [P, GB, D])
        neg_mean = sb("neg_mean", [P, GB])
        var = sb("var", [P, GB])
        std = sb("std", [P, GB])
        inv_std = sb("inv_std", [P, GB])
        out_sb = sb("out_sb", [P, GB, D])

        hT_ps = ps("hT_ps", [P, HALF])
        xT_ps = ps("xT_ps", [P, HALF])
        z_ps = ps("z_ps", [P, 2, 2, HB, D])
        deg_ps = ps("deg_ps", [P, 512])

        x_landed = [sem(f"x_landed{i}") for i in range(XPARTS)]
        weights_landed = sem("weights_landed")
        consts_set = sem("consts_set")
        chunk_landed = [sem(f"chunk_landed{s}") for s in range(SLOTS)]
        chunk_multiplied = sem("chunk_multiplied")
        chunk_summed = sem("chunk_summed")
        x_group_staged = sem("x_group_staged")
        xT_made = sem("xT_made")
        xT_copied = sem("xT_copied")
        hT_copied = sem("hT_copied")
        deg_made = sem("deg_made")
        z_made = sem("z_made")
        tail_step = sem("tail_step")
        relu_made = sem("relu_made")
        norm_made = sem("norm_made")
        std_made = sem("std_made")
        out_stored = sem("out_stored")

        def wide(stat):
            return stat[:, :].unsqueeze(2).broadcast_to([P, GB, D])

        z_self = z_ps[:, :, 0, :, :]
        z_neigh = z_ps[:, :, 1, :, :]

        def halves(t):
            return t[:, :, :].rearrange("p (h k) d -> p h k d", h=2)

        def wide_halves(stat):
            return stat[:, :].rearrange("p (h k) -> p h k", h=2).unsqueeze(3).broadcast_to([P, 2, HB, D])

        (DEG, INV_DEG, SCALED, Z, SQUARE, NORM_SQ, NORM_MAX, INV_NORM, UNIT, Y, SUM, NEG_MEAN,
         CENTRED, SQUARE2, VAR, INV_STD, OUT) = range(1, 18)
        STEPS = OUT

        block = ctx.enter_context(nc.Block())

        @block.sync
        def _(sp):
            for s in range(SLOTS):
                sp.dma_start(ring[:, s, :], adj_chunks[s]).then_inc(chunk_landed[s], 16)
            with sp.Fori(1, G * PASSES) as r:
                for s in range(SLOTS):
                    read = sp.snap(r * SLOTS + (s + 1 - SLOTS))
                    sp.wait_ge(chunk_multiplied, read)
                    sp.wait_ge(chunk_summed, read)
                    src = adj_chunks[bass.ds(r * SLOTS + s, 1)].rearrange("o p n -> (o p) n")
                    sp.dma_start(ring[:, s, :], src).then_inc(chunk_landed[s], 16)

        @block.gpsimd
        def _(pool):
            pool.memset(ones[:, :], 1.0).then_inc(consts_set, 1)
            pool.memset(ln_eps[:, :], LN_EPS).then_inc(consts_set, 1)

        @block.scalar
        def _(act):
            step = NB // XPARTS
            for i in range(XPARTS):
                act.dma_start(x_sb[:, i * step:(i + 1) * step, :],
                              x_nodes[:, i * step:(i + 1) * step, :]).then_inc(x_landed[i], 16)
            act.dma_start(identity[:, :], ident).then_inc(weights_landed, 16)
            for h in range(2):
                rows = slice(h * D, (h + 1) * D)
                act.dma_start(w_self[rows, :], w[0:D, :]).then_inc(weights_landed, 16)
                act.dma_start(w_neigh[rows, :], w[D:2 * D, :]).then_inc(weights_landed, 16)
                for k in range(HB):
                    act.dma_start(bias_row[h * D:h * D + 1, k, :],
                                  b.rearrange("(o d) -> o d", o=1)).then_inc(weights_landed, 16)
            for i in range(XPARTS):
                act.wait_ge(x_landed[i], 16)
            act.wait_ge(consts_set, 2)
            with act.Fori(0, G) as g:
                nc.scalar.activation(x_group[:, :, :], x_sb[:, bass.ds(g * GB, GB), :],
                                     ACT.Copy).then_inc(x_group_staged, 1)
                act.wait_ge(xT_made, g + 1)
                nc.scalar.activation(xT[:, :], xT_ps[:, :], ACT.Copy).then_inc(xT_copied, 1)
                act.wait_ge(chunk_multiplied, (g + 1) * CHUNKS)
                nc.scalar.activation(hT[:, :], hT_ps[:, :], ACT.Copy).then_inc(hT_copied, 1)
                act.wait_ge(tail_step, g * STEPS + Z)
                nc.scalar.activation(relu[:, :, :], z[:, :, :], ACT.Relu).then_inc(relu_made, 1)
                act.wait_ge(tail_step, g * STEPS + NORM_SQ)
                nc.scalar.activation(norm[:, :], norm_sq[:, :], ACT.Sqrt).then_inc(norm_made, 1)
                act.wait_ge(tail_step, g * STEPS + VAR)
                nc.scalar.activation(std[:, :], var[:, :], ACT.Sqrt, bias=ln_eps[:, 0:1],
                                     scale=1.0 / D).then_inc(std_made, 1)
                act.wait_ge(tail_step, g * STEPS + OUT)
                act.dma_start(out_nodes[:, bass.ds(g * GB, GB), :], out_sb[:, :, :]).then_inc(out_stored, 16)
                act.wait_ge(out_stored, (g + 1) * 16)

        @block.vector
        def _(dve):
            with dve.Fori(0, G) as g:
                for c in range(1, CHUNKS):
                    if c == 1:
                        dve.wait_ge(chunk_landed[0], g * (16 * PASSES) + 16)
                    dve.wait_ge(chunk_landed[c % SLOTS], g * (16 * PASSES) + 16 * (c // SLOTS + 1))
                    if c == 1:
                        nc.vector.tensor_tensor(part_deg[:, :], ring[:, 0, :], ring[:, 1, :],
                                                ALU.add).then_inc(chunk_summed, 2)
                    else:
                        dve.wait_ge(chunk_summed, g * CHUNKS + c)
                        nc.vector.tensor_tensor(part_deg[:, :], part_deg[:, :], ring[:, c % SLOTS, :],
                                                ALU.add).then_inc(chunk_summed, 1)

                def done(ins, step):
                    ins.then_inc(tail_step, 1)
                    dve.wait_ge(tail_step, g * STEPS + step)

                dve.wait_ge(deg_made, g + 1)
                done(nc.vector.tensor_scalar(deg[:, :], deg_ps[:, 0:GB], 1.0, 1.0, ALU.add, ALU.max), DEG)
                done(nc.vector.reciprocal(inv_deg[:, :], deg[:, :]), INV_DEG)
                dve.wait_ge(z_made, g + 1)
                done(nc.vector.tensor_tensor(halves(z), z_neigh, wide_halves(inv_deg), ALU.mult), SCALED)
                done(nc.vector.tensor_tensor(halves(z), halves(z), z_self, ALU.add), Z)
                done(nc.vector.scalar_tensor_tensor(out=square[:, :, :], in0=z[:, :, :], scalar=0.0,
                                                    in1=z[:, :, :], op0=ALU.max, op1=ALU.mult), SQUARE)
                done(nc.vector.tensor_reduce(norm_sq[:, :], square[:, :, :], AX_X, ALU.add), NORM_SQ)
                dve.wait_ge(norm_made, g + 1)
                done(nc.vector.tensor_scalar(norm[:, :], norm[:, :], L2_EPS, None, ALU.max), NORM_MAX)
                done(nc.vector.reciprocal(inv_norm[:, :], norm[:, :]), INV_NORM)
                dve.wait_ge(relu_made, g + 1)
                done(nc.vector.tensor_tensor(y[:, :, :], relu[:, :, :], wide(inv_norm), ALU.mult), UNIT)
                done(nc.vector.tensor_tensor(y[:, :, :], y[:, :, :], x_group[:, :, :], ALU.add), Y)
                done(nc.vector.tensor_reduce(neg_mean[:, :], y[:, :, :], AX_X, ALU.add), SUM)
                done(nc.vector.tensor_scalar(neg_mean[:, :], neg_mean[:, :], -1.0 / D, None, ALU.mult), NEG_MEAN)
                done(nc.vector.tensor_tensor(y[:, :, :], y[:, :, :], wide(neg_mean), ALU.add), CENTRED)
                done(nc.vector.tensor_tensor(square[:, :, :], y[:, :, :], y[:, :, :], ALU.mult), SQUARE2)
                done(nc.vector.tensor_reduce(var[:, :], square[:, :, :], AX_X, ALU.add), VAR)
                dve.wait_ge(std_made, g + 1)
                done(nc.vector.reciprocal(inv_std[:, :], std[:, :]), INV_STD)
                done(nc.vector.tensor_tensor(out_sb[:, :, :], y[:, :, :], wide(inv_std), ALU.mult), OUT)

        @block.tensor
        def _(pe):
            def half_of(k):
                h = k // HB
                return slice(h * D, (h + 1) * D), slice((k % HB) * P, (k % HB + 1) * P)

            pe.wait_ge(consts_set, 2)
            pe.wait_ge(weights_landed, 16 * (5 + 2 * HB))
            for i in range(XPARTS):
                pe.wait_ge(x_landed[i], 16)
            with pe.Fori(0, G) as g:
                for c in range(CHUNKS):
                    pe.wait_ge(chunk_landed[c % SLOTS], g * (16 * PASSES) + 16 * (c // SLOTS + 1))
                    for jj in range(JB):
                        j = c * JB + jj
                        for h in range(2):
                            last = nc.tensor.matmul(
                                hT_ps[h * D:(h + 1) * D, :], x_sb[:, j, :],
                                ring[:, c % SLOTS, jj * GC + h * HALF:jj * GC + (h + 1) * HALF],
                                start=(j == 0), stop=(j == NB - 1))
                    last.then_inc(chunk_multiplied, 1)
                    if c == CHUNKS // 2:
                        pe.wait_ge(x_group_staged, g + 1)
                        for k in range(GB):
                            rows, cols = half_of(k)
                            last = nc.tensor.matmul(xT_ps[rows, cols], x_group[:, k, :], identity[:, :],
                                                    start=True, stop=True)
                        last.then_inc(xT_made, 1)
                    if c == CHUNKS // 2 + 1:
                        pe.wait_ge(xT_copied, g + 1)
                        for h in range(2):
                            nc.tensor.matmul(z_ps[:, h, 0, :, :], ones[h * D:h * D + 1, :],
                                             bias_row[h * D:h * D + 1, :, :], start=True, stop=False,
                                             skip_group_check=True)
                        for k in range(GB):
                            rows, cols = half_of(k)
                            for part, weight in ((0, w_self), (1, w_neigh)):
                                nc.tensor.matmul(z_ps[:, k // HB, part, k % HB, :], xT[rows, cols], weight[rows, :],
                                                 start=False, stop=False, skip_group_check=True)
                pe.wait_ge(chunk_summed, (g + 1) * CHUNKS)
                for k in range(GB):
                    for jj in range(JB):
                        last = nc.tensor.matmul(deg_ps[:, k:k + 1], part_deg[:, jj * GC + k * P:jj * GC + (k + 1) * P],
                                                ones[:, 0:1], start=(jj == 0), stop=(jj == JB - 1))
                last.then_inc(deg_made, 1)
                pe.wait_ge(hT_copied, g + 1)
                for k in range(GB):
                    rows, cols = half_of(k)
                    last = nc.tensor.matmul(z_ps[:, k // HB, 1, k % HB, :], hT[rows, cols], w_neigh[rows, :],
                                            start=False, stop=(k % HB == HB - 1), skip_group_check=True)
                last.then_inc(z_made, 1)


def kernel(x, adj, L0_gnn_W, L0_gnn_b):
    import concourse.bacc as bacc
    from concourse.bass_utils import run_bass_kernel_spmd

    x, adj, w, b = (np.ascontiguousarray(a) for a in (x, adj, L0_gnn_W, L0_gnn_b))
    chunks = adj.reshape(P, G, GB, P, CHUNKS, JB).transpose(1, 4, 3, 5, 2, 0)
    chunks = np.ascontiguousarray(chunks).reshape(G * CHUNKS, P, JB * GC)
    arrays = {"x": x, "adj_chunks": chunks, "w": w, "b": b, "ident": np.eye(P, dtype=np.float32)}

    nc = bacc.Bacc("TRN2", target_bir_lowering=False, num_devices=1)
    args = [nc.dram_tensor(f"{n}_dram", a.shape, F32, kind="ExternalInput").ap() for n, a in arrays.items()]
    out = nc.dram_tensor("out_dram", (N, D), F32, kind="ExternalOutput").ap()
    gnn_resnorm(nc, *args, out)
    r = run_bass_kernel_spmd(nc, [{f"{n}_dram": a for n, a in arrays.items()}], core_ids=[0])
    return r.results[0]["out_dram"]
```

```python
from contextlib import ExitStack

import numpy as np

import concourse.bass as bass
from concourse import mybir

N = 8192
D = 64
P = 128
NB = N // P
CW = 4096
SLOTS = 8
GB = 8
LOOPED = 6
ENDING = (4, 4)
GROUPS = (GB,) * (1 + LOOPED) + ENDING
BASE = [sum(GROUPS[:i]) for i in range(len(GROUPS))]
CHUNKS = GB * P * NB // CW
XPARTS = 4
PIECES = (2048, 1024, 512, 512)
PIECE_AT = [sum(PIECES[:i]) for i in range(len(PIECES))]
TILES = 4
TW = P // TILES
BANK = 512
L2_EPS = 1e-12
LN_EPS = 1e-5
assert sum(GROUPS) == NB and CHUNKS % SLOTS == 0 and LOOPED % 2 == 0 and sum(PIECES) == CW

F32 = mybir.dt.float32
ALU = mybir.AluOpType
ACT = mybir.ActivationFunctionType
AX_X = mybir.AxisListType.X

TAIL_STEPS = ("DEG", "INV_DEG", "SCALED", "Z", "NORM_MAX", "INV_NORM", "UNIT", "Y", "SUM", "NEG_MEAN",
              "INV_STD", "SHIFT")
LAST_STEPS = ("DEG", "INV_DEG", "SCALED", "Z", "SQUARE", "NORM_SQ", "NORM_MAX", "INV_NORM", "UNIT", "Y", "SUM",
              "CENTRED", "SQUARE2", "VAR", "INV_STD", "OUT")


class Group:

    def __init__(self, index, parity, blocks=GB, base=None, pair=None):
        self.index, self.parity, self.blocks = index, parity, blocks
        self.base = index * GB if base is None else base
        self.cols = blocks * P
        self.half = self.cols // 2
        self.hb = blocks // 2
        self.jb = CW // self.cols
        self.chunks = NB // self.jb
        self.first = self.base * (CHUNKS // GB)
        looped = blocks == GB
        self.passes = index * (CHUNKS // SLOTS) if looped else self.first // SLOTS
        self.phase = 0 if looped else self.first % SLOTS

        self.earlier = (index - parity) // 2 if isinstance(index, int) else pair
        self.last = isinstance(index, int) and index == len(GROUPS) - 1

    def step(self, name):
        steps = LAST_STEPS if self.last else TAIL_STEPS
        return self.index * len(TAIL_STEPS) + (steps.index(name) + 1)

    def slot(self, c):
        return (self.phase + c) % SLOTS

    def landings(self, c):
        return self.passes * 16 + 16 * ((self.phase + c) // SLOTS + 1)

    def half_of(self, k):
        h, k = divmod(k, self.hb)
        return slice(h * D, (h + 1) * D), slice(k * P, (k + 1) * P)


def gnn_resnorm(nc: bass.Bass, x, adj_chunks, w, b, out):
    x_nodes = x.rearrange("(p b) d -> p b d", b=NB)
    out_nodes = out.rearrange("(p b) d -> p b d", b=NB)
    bias = b.rearrange("(o d) -> o d", o=1)
    ALL_CHUNKS = adj_chunks.shape[0]

    before = Group(0, 0)
    ending = [Group(1 + LOOPED + i, (1 + LOOPED + i) % 2, n, BASE[1 + LOOPED + i]) for i, n in enumerate(ENDING)]
    last_group = ending[-1]

    with ExitStack() as ctx:
        def sb(name, shape):
            return ctx.enter_context(nc.sbuf_tensor(name, shape, F32))

        def ps(name, shape):
            return ctx.enter_context(nc.psum_tensor(name, shape, F32))

        def sem(name):
            return ctx.enter_context(nc.semaphore(name))

        ring = sb("ring", [P, SLOTS, CW])
        x_sb = sb("x_sb", [P, NB, D])
        identity = sb("identity", [P, P])
        w_self = sb("w_self", [P, D])
        w_neigh = sb("w_neigh", [P, D])
        bias_row = sb("bias_row", [P, GB // 2, D])
        ones = sb("ones", [P, P])
        ln_eps = sb("ln_eps", [P, 1])
        part_deg = [sb(f"part_deg{i}", [P, CW]) for i in range(2)]
        x_group = [sb(f"x_group{i}", [P, GB, D]) for i in range(2)]
        xT = sb("xT", [P, GB // 2 * P])
        hT = sb("hT", [P, GB // 2 * P])
        deg = sb("deg", [P, GB])
        inv_deg = sb("inv_deg", [P, GB])
        z = sb("z", [P, GB, D])
        relu = sb("relu", [P, GB, D])
        square = sb("square", [P, GB, D])
        norm_sq = sb("norm_sq", [P, GB])
        norm = sb("norm", [P, GB])
        inv_norm = sb("inv_norm", [P, GB])
        y = sb("y", [P, GB, D])
        total = sb("total", [P, GB])
        neg_mean = sb("neg_mean", [P, GB])
        var = sb("var", [P, GB])
        std = sb("std", [P, GB])
        inv_std = sb("inv_std", [P, GB])
        shift = sb("shift", [P, GB])
        deg_rows = sb("deg_rows", [P, GB * P])
        copies = sb("copies", [P, 1])
        out_sb = [sb(f"out_sb{i}", [P, GB, D]) for i in range(2)]

        hT_ps = [ps(f"hT_ps{i}", [P, BANK]) for i in range(2)]
        xT_ps = ps("xT_ps", [P, BANK])
        z_ps = ps("z_ps", [P, 2, 2, GB // 2, D])
        deg_rows_ps = ps("deg_rows_ps", [P, GB * P])
        deg_ps = ps("deg_ps", [P, BANK])

        x_landed = [sem(f"x_landed{i}") for i in range(XPARTS)]
        weights_landed = sem("weights_landed")
        consts_set = sem("consts_set")
        chunk_landed = [sem(f"chunk_landed{s}") for s in range(SLOTS)]
        piece_landed = [sem(f"piece_landed{i}") for i in range(len(PIECES))]
        chunk_multiplied = sem("chunk_multiplied")
        chunk_summed = sem("chunk_summed")
        sums_folded = sem("sums_folded")
        piece_summed = sem("piece_summed")
        x_group_staged = sem("x_group_staged")
        xT_made = sem("xT_made")
        xT_copied = sem("xT_copied")
        hT_copied = sem("hT_copied")
        deg_rows_made = sem("deg_rows_made")
        deg_rows_copied = sem("deg_rows_copied")
        deg_made = sem("deg_made")
        z_made = sem("z_made")
        tail_step = sem("tail_step")
        relu_made = sem("relu_made")
        norm_sq_made = sem("norm_sq_made")
        norm_made = sem("norm_made")
        var_made = sem("var_made")
        std_made = sem("std_made")
        out_made = sem("out_made")
        out_free = [sem(f"out_free{i}") for i in range(2)]

        WEIGHT_LOADS = 6

        def by_half(t, gr):
            return t[:, 0:gr.blocks, :].rearrange("p (h k) d -> p h k d", h=2)

        def wide(stat, gr):
            return stat[:, 0:gr.blocks].unsqueeze(2).broadcast_to([P, gr.blocks, D])

        def wide_by_half(stat, gr):
            v = stat[:, 0:gr.blocks].rearrange("p (h k) -> p h k", h=2)
            return v.unsqueeze(3).broadcast_to([P, 2, gr.hb, D])

        def each_group(eng, body):
            body(before, None)
            with eng.Fori(0, LOOPED // 2) as r:
                groups = [Group(r * 2 + i, i % 2, pair=r + i // 2) for i in range(3)]
                body(groups[1], groups[0])
                body(groups[2], groups[1])
            prev = Group(LOOPED, LOOPED % 2)
            for gr in ending:
                body(gr, prev)
                prev = gr

        block = ctx.enter_context(nc.Block())

        @block.sync
        def _(sp):
            ahead = CHUNKS // XPARTS

            def load_x(i):
                part = slice(i * NB // XPARTS, (i + 1) * NB // XPARTS)
                sp.dma_start(x_sb[:, part, :], x_nodes[:, part, :]).then_inc(x_landed[i], 16)

            for s in range(SLOTS):
                if s % ahead == 0:
                    load_x(s // ahead)
                sp.dma_start(ring[:, s, :], adj_chunks[s]).then_inc(chunk_landed[s], 16)
            for i in range(SLOTS // ahead, XPARTS):
                load_x(i)
            with sp.Fori(1, ALL_CHUNKS // SLOTS - 1) as r:
                for s in range(SLOTS):
                    read = sp.snap(r * SLOTS + (s + 1 - SLOTS))
                    sp.wait_ge(chunk_multiplied, read)
                    sp.wait_ge(chunk_summed, read)
                    src = adj_chunks[bass.ds(r * SLOTS + s, 1)].rearrange("o p n -> (o p) n")
                    sp.dma_start(ring[:, s, :], src).then_inc(chunk_landed[s], 16)
            for c in range(ALL_CHUNKS - SLOTS, ALL_CHUNKS):
                sp.wait_ge(chunk_multiplied, c + 1 - SLOTS)
                sp.wait_ge(chunk_summed, c + 1 - SLOTS)
                if c < ALL_CHUNKS - 1:
                    sp.dma_start(ring[:, c % SLOTS, :], adj_chunks[c]).then_inc(chunk_landed[c % SLOTS], 16)
                else:
                    for i, (at, width) in enumerate(zip(PIECE_AT, PIECES)):
                        cols = slice(at, at + width)
                        sp.dma_start(ring[:, c % SLOTS, cols], adj_chunks[c, :, cols]).then_inc(piece_landed[i], 16)

        @block.gpsimd
        def _(pool):
            pool.memset(ones[:, :], 1.0).then_inc(consts_set, 1)
            pool.memset(ln_eps[:, :], LN_EPS).then_inc(consts_set, 1)
            pool.memset(identity[:, :], 0.0).then_inc(consts_set, 1)
            pool.memset(copies[:, :], 1.0 / TW).then_inc(consts_set, 1)
            pool.wait_ge(consts_set, 4)
            pool.affine_select(out=identity[:, :], in_=identity[:, :], compare_op=ALU.not_equal, fill=1.0,
                               base=0, pattern=[[-1, P]], channel_multiplier=1).then_inc(consts_set, 1)
            for i in range(2):
                pool.memset(out_sb[i][:, :, :], 0.0).then_inc(out_free[i], 16)

        @block.scalar
        def _(act):
            for h in range(2):
                rows = slice(h * D, (h + 1) * D)
                act.dma_start(w_self[rows, :], w[0:D, :]).then_inc(weights_landed, 16)
                act.dma_start(w_neigh[rows, :], w[D:2 * D, :]).then_inc(weights_landed, 16)
                act.dma_start(bias_row[h * D:h * D + 1, :, :],
                              bias.unsqueeze(1).broadcast_to([1, GB // 2, D])).then_inc(weights_landed, 16)
            for i in range(XPARTS):
                act.wait_ge(x_landed[i], 16)
            act.wait_ge(consts_set, 5)

            def tail(gr):
                n = gr.blocks
                act.wait_ge(tail_step, gr.step("Z"))
                nc.scalar.activation(relu[:, 0:n, :], z[:, 0:n, :], ACT.Relu).then_inc(relu_made, 1)
                if not gr.last:
                    act.wait_ge(relu_made, gr.index + 1)
                    for k in range(n):
                        last = nc.scalar.activation(square[:, k, :], relu[:, k, :], ACT.Square,
                                                    accum_out=norm_sq[:, k:k + 1])
                    last.then_inc(norm_sq_made, 1)
                    act.wait_ge(norm_sq_made, gr.index + 1)
                else:
                    act.wait_ge(tail_step, gr.step("NORM_SQ"))
                nc.scalar.activation(norm[:, 0:n], norm_sq[:, 0:n], ACT.Sqrt).then_inc(norm_made, 1)
                if not gr.last:
                    act.wait_ge(tail_step, gr.step("NEG_MEAN"))
                    for k in range(n):
                        last = nc.scalar.activation(square[:, k, :], y[:, k, :], ACT.Square,
                                                    bias=neg_mean[:, k:k + 1], accum_out=var[:, k:k + 1])
                    last.then_inc(var_made, 1)
                    act.wait_ge(var_made, gr.index + 1)
                else:
                    act.wait_ge(tail_step, gr.step("VAR"))
                nc.scalar.activation(std[:, 0:n], var[:, 0:n], ACT.Sqrt, bias=ln_eps[:, 0:1],
                                     scale=1.0 / D).then_inc(std_made, 1)
                if not gr.last:
                    act.wait_ge(tail_step, gr.step("SHIFT"))
                    act.wait_ge(out_free[gr.parity], gr.earlier * 16 + 16)
                    for k in range(n):
                        last = nc.scalar.activation(out_sb[gr.parity][:, k, :], y[:, k, :], ACT.Identity,
                                                    bias=shift[:, k:k + 1], scale=inv_std[:, k:k + 1])
                    last.then_inc(out_made, 1)
                    act.wait_ge(out_made, gr.index + 1)
                else:
                    act.wait_ge(tail_step, gr.step("OUT"))
                act.dma_start(out_nodes[:, bass.ds(gr.base, n), :],
                              out_sb[gr.parity][:, 0:n, :]).then_inc(out_free[gr.parity], 16)

            def copy_hT(gr):
                act.wait_ge(chunk_multiplied, gr.first + gr.chunks)
                nc.scalar.activation(hT[:, 0:gr.half], hT_ps[gr.parity][:, 0:gr.half],
                                     ACT.Copy).then_inc(hT_copied, 1)

            def copy_deg_rows(gr):
                act.wait_ge(deg_rows_made, gr.index + 1)
                nc.scalar.activation(deg_rows[:, 0:gr.cols], deg_rows_ps[:, 0:gr.cols],
                                     ACT.Copy).then_inc(deg_rows_copied, 1)

            def body(gr, prev):
                nc.scalar.activation(x_group[gr.parity][:, 0:gr.blocks, :], x_sb[:, bass.ds(gr.base, gr.blocks), :],
                                     ACT.Copy).then_inc(x_group_staged, 1)
                if prev:
                    copy_hT(prev)
                    copy_deg_rows(prev)
                    tail(prev)
                act.wait_ge(xT_made, gr.index + 1)
                nc.scalar.activation(xT[:, 0:gr.half], xT_ps[:, 0:gr.half], ACT.Copy).then_inc(xT_copied, 1)

            each_group(act, body)
            copy_hT(last_group)
            tail(last_group)
            for gr in ending[-2:]:
                act.wait_ge(out_free[gr.parity], gr.earlier * 16 + 32)

        @block.vector
        def _(dve):
            def add_chunk(gr, c):
                sums = part_deg[gr.parity]
                if c == 1:
                    dve.wait_ge(chunk_landed[gr.slot(0)], gr.landings(0))
                dve.wait_ge(chunk_landed[gr.slot(c)], gr.landings(c))
                if c == 1:
                    nc.vector.tensor_tensor(sums[:, :], ring[:, gr.slot(0), :], ring[:, gr.slot(1), :],
                                            ALU.add).then_inc(chunk_summed, 2)
                else:
                    dve.wait_ge(chunk_summed, gr.first + c)
                    nc.vector.tensor_tensor(sums[:, :], sums[:, :], ring[:, gr.slot(c), :],
                                            ALU.add).then_inc(chunk_summed, 1)

            def add_pieces(gr):
                sums, width, folds = part_deg[gr.parity], CW, 0
                dve.wait_ge(chunk_summed, gr.first + gr.chunks - 1)
                for i, (at, piece) in enumerate(zip(PIECE_AT, PIECES)):
                    if i:
                        dve.wait_ge(piece_summed, i)
                    while width > piece:
                        width //= 2
                        folds += 1
                        nc.vector.tensor_tensor(sums[:, 0:width], sums[:, 0:width], sums[:, width:2 * width],
                                                ALU.add).then_inc(sums_folded, 1)
                        dve.wait_ge(sums_folded, folds)
                    dve.wait_ge(piece_landed[i], 16)
                    nc.vector.tensor_tensor(sums[:, 0:width], sums[:, 0:width],
                                            ring[:, gr.slot(gr.chunks - 1), at:at + width],
                                            ALU.add).then_inc(piece_summed, 1)

            def done(ins, gr, name):
                ins.then_inc(tail_step, 1)
                dve.wait_ge(tail_step, gr.step(name))

            def linear(gr):
                n = gr.blocks
                z_self, z_neigh = (z_ps[:, :, part, 0:gr.hb, :] for part in range(2))
                dve.wait_ge(deg_made, gr.index + 1)
                done(nc.vector.tensor_scalar(deg[:, 0:n], deg_ps[:, 0:n], 1.0, 1.0, ALU.add, ALU.max), gr, "DEG")
                done(nc.vector.reciprocal(inv_deg[:, 0:n], deg[:, 0:n]), gr, "INV_DEG")
                dve.wait_ge(z_made, gr.index + 1)
                done(nc.vector.tensor_tensor(by_half(z, gr), z_neigh, wide_by_half(inv_deg, gr), ALU.mult),
                     gr, "SCALED")
                done(nc.vector.tensor_tensor(by_half(z, gr), by_half(z, gr), z_self, ALU.add), gr, "Z")

            def residual(gr):
                n = gr.blocks
                zs, ys = z[:, 0:n, :], y[:, 0:n, :]
                if gr.last:
                    done(nc.vector.scalar_tensor_tensor(out=square[:, 0:n, :], in0=zs, scalar=0.0, in1=zs,
                                                        op0=ALU.max, op1=ALU.mult), gr, "SQUARE")
                    done(nc.vector.tensor_reduce(norm_sq[:, 0:n], square[:, 0:n, :], AX_X, ALU.add), gr, "NORM_SQ")
                dve.wait_ge(norm_made, gr.index + 1)
                done(nc.vector.tensor_scalar(norm[:, 0:n], norm[:, 0:n], L2_EPS, None, ALU.max), gr, "NORM_MAX")
                done(nc.vector.reciprocal(inv_norm[:, 0:n], norm[:, 0:n]), gr, "INV_NORM")
                dve.wait_ge(relu_made, gr.index + 1)
                done(nc.vector.tensor_tensor(ys, relu[:, 0:n, :], wide(inv_norm, gr), ALU.mult), gr, "UNIT")
                done(nc.vector.tensor_tensor(ys, ys, x_group[gr.parity][:, 0:n, :], ALU.add), gr, "Y")
                done(nc.vector.tensor_reduce(total[:, 0:n], ys, AX_X, ALU.add), gr, "SUM")
                if not gr.last:
                    done(nc.vector.tensor_scalar(neg_mean[:, 0:n], total[:, 0:n], -1.0 / D, None, ALU.mult),
                         gr, "NEG_MEAN")

            def layer_norm(gr):
                n = gr.blocks
                ys, sq = y[:, 0:n, :], square[:, 0:n, :]
                if gr.last:
                    done(nc.vector.scalar_tensor_tensor(out=ys, in0=wide(total, gr), scalar=-1.0 / D, in1=ys,
                                                        op0=ALU.mult, op1=ALU.add), gr, "CENTRED")
                    done(nc.vector.tensor_tensor(sq, ys, ys, ALU.mult), gr, "SQUARE2")
                    done(nc.vector.tensor_reduce(var[:, 0:n], sq, AX_X, ALU.add), gr, "VAR")
                dve.wait_ge(std_made, gr.index + 1)
                done(nc.vector.reciprocal(inv_std[:, 0:n], std[:, 0:n]), gr, "INV_STD")
                if not gr.last:
                    done(nc.vector.tensor_tensor(shift[:, 0:n], neg_mean[:, 0:n], inv_std[:, 0:n], ALU.mult),
                         gr, "SHIFT")
                else:
                    dve.wait_ge(out_free[gr.parity], gr.earlier * 16 + 16)
                    done(nc.vector.tensor_tensor(out_sb[gr.parity][:, 0:n, :], ys, wide(inv_std, gr), ALU.mult),
                         gr, "OUT")

            def body(gr, prev):
                for c in range(1, gr.chunks - (gr.last)):
                    add_chunk(gr, c)
                    for at, stage in ((gr.chunks // 4, linear), (3 * gr.chunks // 8, residual),
                                      (gr.chunks // 2, layer_norm)):
                        if prev and c == at:
                            stage(prev)
                if gr.last:
                    add_pieces(gr)

            each_group(dve, body)
            linear(last_group)
            residual(last_group)
            layer_norm(last_group)

        @block.tensor
        def _(pe):
            def multiply(gr, c, jjs):
                for jj in jjs:
                    j = c * gr.jb + jj
                    for h in range(2):
                        at = jj * gr.cols + h * gr.half
                        last = nc.tensor.matmul(
                            hT_ps[gr.parity][h * D:(h + 1) * D, 0:gr.half], x_sb[:, j, :],
                            ring[:, gr.slot(c), at:at + gr.half], start=(j == 0), stop=(j == NB - 1))
                return last

            def transpose_x(gr):
                pe.wait_ge(x_group_staged, gr.index + 1)
                for k in range(gr.blocks):
                    rows, cols = gr.half_of(k)
                    last = nc.tensor.matmul(xT_ps[rows, cols], x_group[gr.parity][:, k, :], identity[:, :],
                                            start=True, stop=True)
                last.then_inc(xT_made, 1)

            def self_part(gr, prev):
                pe.wait_ge(xT_copied, gr.index + 1)
                if prev:
                    pe.wait_ge(tail_step, prev.step("Z"))
                for h in range(2):
                    nc.tensor.matmul(z_ps[:, h, 0, 0:gr.hb, :], ones[h * D:h * D + 1, :],
                                     bias_row[h * D:h * D + 1, 0:gr.hb, :], start=True, stop=False,
                                     skip_group_check=True)
                for k in range(gr.blocks):
                    rows, cols = gr.half_of(k)
                    for part, weight in ((0, w_self), (1, w_neigh)):
                        nc.tensor.matmul(z_ps[:, k // gr.hb, part, k % gr.hb, :], xT[rows, cols], weight[rows, :],
                                         start=False, stop=False, skip_group_check=True)

            def degree_rows(gr):
                sums = part_deg[gr.parity]
                pe.wait_ge(chunk_summed, gr.first + gr.chunks)
                for at in range(0, gr.cols, BANK):
                    for jj in range(gr.jb):
                        rows = slice(jj % TILES * TW, (jj % TILES + 1) * TW)
                        col = jj * gr.cols + at
                        last = nc.tensor.matmul(deg_rows_ps[rows, at:at + BANK], ones[:, 0:TW],
                                                sums[:, col:col + BANK],
                                                start=(jj < TILES), stop=(jj >= gr.jb - TILES))
                last.then_inc(deg_rows_made, 1)

            def degrees(gr):
                pe.wait_ge(deg_rows_copied, gr.index + 1)
                for k in range(gr.blocks):
                    last = nc.tensor.matmul(deg_ps[:, k:k + 1], deg_rows[:, k * P:(k + 1) * P], copies[:, 0:1],
                                            start=True, stop=True)
                last.then_inc(deg_made, 1)

            def last_degrees(gr):
                sums, parts = part_deg[gr.parity], PIECES[-1] // gr.cols
                pe.wait_ge(piece_summed, len(PIECES))
                for k in range(gr.blocks):
                    for jj in range(parts):
                        at = jj * gr.cols + k * P
                        last = nc.tensor.matmul(deg_ps[:, k:k + 1], sums[:, at:at + P], ones[:, 0:1],
                                                start=(jj == 0), stop=(jj == parts - 1))
                last.then_inc(deg_made, 1)

            def neighbour_part(gr):
                pe.wait_ge(hT_copied, gr.index + 1)
                for k in range(gr.blocks):
                    rows, cols = gr.half_of(k)
                    last = nc.tensor.matmul(z_ps[:, k // gr.hb, 1, k % gr.hb, :], hT[rows, cols], w_neigh[rows, :],
                                            start=False, stop=(k % gr.hb == gr.hb - 1), skip_group_check=True)
                last.then_inc(z_made, 1)

            def body(gr, prev):
                for c in range(gr.chunks):
                    if c == gr.chunks // 2:
                        transpose_x(gr)
                    if c == 3 * gr.chunks // 4:
                        if not prev:
                            pe.wait_ge(weights_landed, 16 * WEIGHT_LOADS)
                        self_part(gr, prev)
                    if not prev and c % (CHUNKS // XPARTS) == 0:
                        pe.wait_ge(x_landed[c // (CHUNKS // XPARTS)], 16)
                    if gr.last and c == gr.chunks - 1:
                        for i, (at, width) in enumerate(zip(PIECE_AT, PIECES)):
                            pe.wait_ge(piece_landed[i], 16)
                            last = multiply(gr, c, range(at // gr.cols, (at + width) // gr.cols))
                    else:
                        pe.wait_ge(chunk_landed[gr.slot(c)], gr.landings(c))
                        last = multiply(gr, c, range(gr.jb))
                    last.then_inc(chunk_multiplied, 1)
                    if c == gr.chunks // 8 and prev:
                        degree_rows(prev)
                        neighbour_part(prev)
                        degrees(prev)

            pe.wait_ge(consts_set, 5)
            each_group(pe, body)
            last_degrees(last_group)
            neighbour_part(last_group)


def kernel(x, adj, L0_gnn_W, L0_gnn_b):
    import concourse.bacc as bacc
    from concourse.bass_utils import run_bass_kernel_spmd

    x, adj, w, b = (np.ascontiguousarray(a) for a in (x, adj, L0_gnn_W, L0_gnn_b))
    chunks = []
    for base, n in zip(BASE, GROUPS):
        jb = CW // (n * P)
        rows = adj.reshape(P, NB, N)[:, base:base + n].reshape(P, n, P, NB // jb, jb)
        chunks.append(rows.transpose(3, 2, 4, 1, 0).reshape(NB // jb, P, CW))
    arrays = {"x": x, "adj_chunks": np.concatenate(chunks), "w": w, "b": b}

    nc = bacc.Bacc("TRN2", target_bir_lowering=False, num_devices=1)
    args = [nc.dram_tensor(f"{n}_dram", a.shape, F32, kind="ExternalInput").ap() for n, a in arrays.items()]
    out = nc.dram_tensor("out_dram", (N, D), F32, kind="ExternalOutput").ap()
    gnn_resnorm(nc, *args, out)
    r = run_bass_kernel_spmd(nc, [{f"{n}_dram": a for n, a in arrays.items()}], core_ids=[0])
    return r.results[0]["out_dram"]
```

```python
from contextlib import ExitStack

import numpy as np

import concourse.bass as bass
from concourse import mybir

N = 8192
D = 64
P = 128
NB = N // P
CW = 4096
SLOTS = 8
GB = 8
LOOPED = 6
ENDING = (4, 4)
GROUPS = (GB,) * (1 + LOOPED) + ENDING
BASE = [sum(GROUPS[:i]) for i in range(len(GROUPS))]
CHUNKS = GB * P * NB // CW
XPARTS = 4
TILES = 4
TW = P // TILES
BANK = 512

PIECES = (2048, 2048, 2048, 1024, 512, 512)
PIECE_AT = [sum(PIECES[:i]) for i in range(len(PIECES))]
PIECED = 2
TENSOR_SUMS = 3


def piece_plan(nodes):
    plan, width = [], CW
    while width > nodes:
        width //= 2
        plan.append(("fold", width, None, None))
    for i in range(TENSOR_SUMS, len(PIECES)):
        if i == len(PIECES) - 1:
            plan.append(("rows", width, None, None))
        plan += [("add", width, i, col) for col in range(PIECE_AT[i], PIECE_AT[i] + PIECES[i], width)]
    return plan


PIECE_PLAN = piece_plan(ENDING[-1] * P)
L2_EPS = 1e-12
LN_EPS = 1e-5
assert sum(GROUPS) == NB and CHUNKS % SLOTS == 0 and LOOPED % 2 == 0 and sum(PIECES) == PIECED * CW

F32 = mybir.dt.float32
ALU = mybir.AluOpType
ACT = mybir.ActivationFunctionType
AX_X = mybir.AxisListType.X

TAIL_STEPS = ("DEG", "INV_DEG", "SCALED", "Z", "NORM_MAX", "INV_NORM", "UNIT", "Y", "SUM", "NEG_MEAN",
              "INV_STD", "SHIFT")
LAST_STEPS = ("DEG", "INV_DEG", "SCALED", "Z", "SQUARE", "NORM_SQ", "NORM_MAX", "INV_NORM", "UNIT", "Y", "SUM",
              "CENTRED", "SQUARE2", "VAR", "INV_STD", "OUT")


class Group:

    def __init__(self, index, parity, blocks=GB, base=None, pair=None):
        self.index, self.parity, self.blocks = index, parity, blocks
        self.base = index * GB if base is None else base
        self.cols = blocks * P
        self.half = self.cols // 2
        self.hb = blocks // 2
        self.jb = CW // self.cols
        self.chunks = NB // self.jb
        self.first = self.base * (CHUNKS // GB)
        looped = blocks == GB
        self.passes = index * (CHUNKS // SLOTS) if looped else self.first // SLOTS
        self.phase = 0 if looped else self.first % SLOTS
        self.earlier = (index - parity) // 2 if isinstance(index, int) else pair
        self.last = isinstance(index, int) and index == len(GROUPS) - 1

    def step(self, name):
        steps = LAST_STEPS if self.last else TAIL_STEPS
        return self.index * len(TAIL_STEPS) + (steps.index(name) + 1)

    def slot(self, c):
        return (self.phase + c) % SLOTS

    def piece(self, at):
        return self.slot(self.chunks - PIECED + at // CW), at % CW

    def landings(self, c):
        return self.passes * 16 + 16 * ((self.phase + c) // SLOTS + 1)

    def half_of(self, k):
        h, k = divmod(k, self.hb)
        return slice(h * D, (h + 1) * D), slice(k * P, (k + 1) * P)


def gnn_resnorm(nc: bass.Bass, x, adj_chunks, w, b, out):
    x_nodes = x.rearrange("(p b) d -> p b d", b=NB)
    out_nodes = out.rearrange("(p b) d -> p b d", b=NB)
    bias = b.rearrange("(o d) -> o d", o=1)
    ALL_CHUNKS = adj_chunks.shape[0]

    first_group = Group(0, 0)
    ending = [Group(1 + LOOPED + i, (1 + LOOPED + i) % 2, n, BASE[1 + LOOPED + i]) for i, n in enumerate(ENDING)]
    last_group = ending[-1]

    with ExitStack() as ctx:
        def sb(name, shape):
            return ctx.enter_context(nc.sbuf_tensor(name, shape, F32))

        def ps(name, shape):
            return ctx.enter_context(nc.psum_tensor(name, shape, F32))

        def sem(name):
            return ctx.enter_context(nc.semaphore(name))

        ring = sb("ring", [P, SLOTS, CW])
        x_sb = sb("x_sb", [P, NB, D])
        identity = sb("identity", [P, P])
        w_self = sb("w_self", [P, D])
        w_neigh = sb("w_neigh", [P, D])
        bias_row = sb("bias_row", [P, GB // 2, D])
        ones = sb("ones", [P, P])
        ln_eps = sb("ln_eps", [P, 1])
        part_deg = [sb(f"part_deg{i}", [P, CW]) for i in range(2)]
        x_group = [sb(f"x_group{i}", [P, GB, D]) for i in range(2)]
        xT = sb("xT", [P, GB // 2 * P])
        hT = sb("hT", [P, GB // 2 * P])
        deg = sb("deg", [P, GB])
        inv_deg = sb("inv_deg", [P, GB])
        z = sb("z", [P, GB, D])
        relu = sb("relu", [P, GB, D])
        square = sb("square", [P, GB, D])
        norm_sq = sb("norm_sq", [P, GB])
        norm = sb("norm", [P, GB])
        inv_norm = sb("inv_norm", [P, GB])
        y = sb("y", [P, GB, D])
        total = sb("total", [P, GB])
        neg_mean = sb("neg_mean", [P, GB])
        var = sb("var", [P, GB])
        std = sb("std", [P, GB])
        inv_std = sb("inv_std", [P, GB])
        shift = sb("shift", [P, GB])
        deg_rows = sb("deg_rows", [P, GB * P])
        copies = sb("copies", [P, 1])
        out_sb = [sb(f"out_sb{i}", [P, GB, D]) for i in range(2)]

        hT_ps = [ps(f"hT_ps{i}", [P, BANK]) for i in range(2)]
        xT_ps = ps("xT_ps", [P, BANK])
        z_ps = ps("z_ps", [P, 2, 2, GB // 2, D])
        deg_rows_ps = ps("deg_rows_ps", [P, GB * P])
        deg_ps = ps("deg_ps", [P, BANK])

        x_landed = [sem(f"x_landed{i}") for i in range(XPARTS)]
        weights_landed = sem("weights_landed")
        consts_set = sem("consts_set")
        chunk_landed = [sem(f"chunk_landed{s}") for s in range(SLOTS)]
        piece_landed = [sem(f"piece_landed{i}") for i in range(len(PIECES))]
        chunk_multiplied = sem("chunk_multiplied")
        chunk_summed = sem("chunk_summed")
        piece_step = sem("piece_step")
        x_group_staged = sem("x_group_staged")
        xT_made = sem("xT_made")
        xT_copied = sem("xT_copied")
        hT_copied = sem("hT_copied")
        deg_rows_made = sem("deg_rows_made")
        deg_rows_copied = sem("deg_rows_copied")
        deg_made = sem("deg_made")
        z_made = sem("z_made")
        tail_step = sem("tail_step")
        relu_made = sem("relu_made")
        norm_sq_made = sem("norm_sq_made")
        norm_made = sem("norm_made")
        var_made = sem("var_made")
        std_made = sem("std_made")
        out_made = sem("out_made")
        out_free = [sem(f"out_free{i}") for i in range(2)]

        WEIGHT_LOADS = 6

        def by_half(t, gr):
            return t[:, 0:gr.blocks, :].rearrange("p (h k) d -> p h k d", h=2)

        def wide(stat, gr):
            return stat[:, 0:gr.blocks].unsqueeze(2).broadcast_to([P, gr.blocks, D])

        def wide_by_half(stat, gr):
            v = stat[:, 0:gr.blocks].rearrange("p (h k) -> p h k", h=2)
            return v.unsqueeze(3).broadcast_to([P, 2, gr.hb, D])

        def each_group(eng, body):
            body(first_group, None)
            with eng.Fori(0, LOOPED // 2) as r:
                groups = [Group(r * 2 + i, i % 2, pair=r + i // 2) for i in range(3)]
                body(groups[1], groups[0])
                body(groups[2], groups[1])
            prev = Group(LOOPED, LOOPED % 2)
            for gr in ending:
                body(gr, prev)
                prev = gr

        block = ctx.enter_context(nc.Block())

        @block.sync
        def _(sp):
            ahead = CHUNKS // XPARTS

            def load_x(i):
                part = slice(i * NB // XPARTS, (i + 1) * NB // XPARTS)
                sp.dma_start(x_sb[:, part, :], x_nodes[:, part, :]).then_inc(x_landed[i], 16)

            for s in range(SLOTS):
                if s % ahead == 0:
                    load_x(s // ahead)
                sp.dma_start(ring[:, s, :], adj_chunks[s]).then_inc(chunk_landed[s], 16)
            for i in range(SLOTS // ahead, XPARTS):
                load_x(i)
            with sp.Fori(1, ALL_CHUNKS // SLOTS - 1) as r:
                for s in range(SLOTS):
                    read = sp.snap(r * SLOTS + (s + 1 - SLOTS))
                    sp.wait_ge(chunk_multiplied, read)
                    sp.wait_ge(chunk_summed, read)
                    src = adj_chunks[bass.ds(r * SLOTS + s, 1)].rearrange("o p n -> (o p) n")
                    sp.dma_start(ring[:, s, :], src).then_inc(chunk_landed[s], 16)
            for c in range(ALL_CHUNKS - SLOTS, ALL_CHUNKS):
                sp.wait_ge(chunk_multiplied, c + 1 - SLOTS)
                sp.wait_ge(chunk_summed, c + 1 - SLOTS)
                if c < ALL_CHUNKS - PIECED:
                    sp.dma_start(ring[:, c % SLOTS, :], adj_chunks[c]).then_inc(chunk_landed[c % SLOTS], 16)
                else:
                    for i, (at, width) in enumerate(zip(PIECE_AT, PIECES)):
                        if at // CW == c - (ALL_CHUNKS - PIECED):
                            cols = slice(at % CW, at % CW + width)
                            sp.dma_start(ring[:, c % SLOTS, cols],
                                         adj_chunks[c, :, cols]).then_inc(piece_landed[i], 16)

        @block.gpsimd
        def _(pool):
            pool.memset(ones[:, :], 1.0).then_inc(consts_set, 1)
            pool.memset(ln_eps[:, :], LN_EPS).then_inc(consts_set, 1)
            pool.memset(identity[:, :], 0.0).then_inc(consts_set, 1)
            pool.memset(copies[:, :], 1.0 / TW).then_inc(consts_set, 1)
            pool.wait_ge(consts_set, 4)
            pool.affine_select(out=identity[:, :], in_=identity[:, :], compare_op=ALU.not_equal, fill=1.0,
                               base=0, pattern=[[-1, P]], channel_multiplier=1).then_inc(consts_set, 1)
            for i in range(2):
                pool.memset(out_sb[i][:, :, :], 0.0).then_inc(out_free[i], 16)

        @block.scalar
        def _(act):
            for h in range(2):
                rows = slice(h * D, (h + 1) * D)
                act.dma_start(w_self[rows, :], w[0:D, :]).then_inc(weights_landed, 16)
                act.dma_start(w_neigh[rows, :], w[D:2 * D, :]).then_inc(weights_landed, 16)
                act.dma_start(bias_row[h * D:h * D + 1, :, :],
                              bias.unsqueeze(1).broadcast_to([1, GB // 2, D])).then_inc(weights_landed, 16)
            for i in range(XPARTS):
                act.wait_ge(x_landed[i], 16)
            act.wait_ge(consts_set, 5)

            def tail(gr):
                n = gr.blocks
                act.wait_ge(tail_step, gr.step("Z"))
                nc.scalar.activation(relu[:, 0:n, :], z[:, 0:n, :], ACT.Relu).then_inc(relu_made, 1)
                if not gr.last:
                    act.wait_ge(relu_made, gr.index + 1)
                    for k in range(n):
                        last = nc.scalar.activation(square[:, k, :], relu[:, k, :], ACT.Square,
                                                    accum_out=norm_sq[:, k:k + 1])
                    last.then_inc(norm_sq_made, 1)
                    act.wait_ge(norm_sq_made, gr.index + 1)
                else:
                    act.wait_ge(tail_step, gr.step("NORM_SQ"))
                nc.scalar.activation(norm[:, 0:n], norm_sq[:, 0:n], ACT.Sqrt).then_inc(norm_made, 1)
                if not gr.last:
                    act.wait_ge(tail_step, gr.step("NEG_MEAN"))
                    for k in range(n):
                        last = nc.scalar.activation(square[:, k, :], y[:, k, :], ACT.Square,
                                                    bias=neg_mean[:, k:k + 1], accum_out=var[:, k:k + 1])
                    last.then_inc(var_made, 1)
                    act.wait_ge(var_made, gr.index + 1)
                else:
                    act.wait_ge(tail_step, gr.step("VAR"))
                nc.scalar.activation(std[:, 0:n], var[:, 0:n], ACT.Sqrt, bias=ln_eps[:, 0:1],
                                     scale=1.0 / D).then_inc(std_made, 1)
                if not gr.last:
                    act.wait_ge(tail_step, gr.step("SHIFT"))
                    act.wait_ge(out_free[gr.parity], gr.earlier * 16 + 16)
                    for k in range(n):
                        last = nc.scalar.activation(out_sb[gr.parity][:, k, :], y[:, k, :], ACT.Identity,
                                                    bias=shift[:, k:k + 1], scale=inv_std[:, k:k + 1])
                    last.then_inc(out_made, 1)
                    act.wait_ge(out_made, gr.index + 1)
                else:
                    act.wait_ge(tail_step, gr.step("OUT"))
                act.dma_start(out_nodes[:, bass.ds(gr.base, n), :],
                              out_sb[gr.parity][:, 0:n, :]).then_inc(out_free[gr.parity], 16)

            def copy_hT(gr):
                act.wait_ge(chunk_multiplied, gr.first + gr.chunks)
                nc.scalar.activation(hT[:, 0:gr.half], hT_ps[gr.parity][:, 0:gr.half],
                                     ACT.Copy).then_inc(hT_copied, 1)

            def copy_deg_rows(gr):
                act.wait_ge(deg_rows_made, gr.index + 1)
                nc.scalar.activation(deg_rows[:, 0:gr.cols], deg_rows_ps[:, 0:gr.cols],
                                     ACT.Copy).then_inc(deg_rows_copied, 1)

            def body(gr, prev):
                nc.scalar.activation(x_group[gr.parity][:, 0:gr.blocks, :], x_sb[:, bass.ds(gr.base, gr.blocks), :],
                                     ACT.Copy).then_inc(x_group_staged, 1)
                act.wait_ge(xT_made, gr.index + 1)
                nc.scalar.activation(xT[:, 0:gr.half], xT_ps[:, 0:gr.half], ACT.Copy).then_inc(xT_copied, 1)
                if prev:
                    copy_hT(prev)
                    copy_deg_rows(prev)
                    tail(prev)

            each_group(act, body)
            copy_hT(last_group)
            tail(last_group)
            for gr in ending[-2:]:
                act.wait_ge(out_free[gr.parity], gr.earlier * 16 + 32)

        @block.vector
        def _(dve):
            def add_chunk(gr, c):
                sums = part_deg[gr.parity]
                if c == 1:
                    dve.wait_ge(chunk_landed[gr.slot(0)], gr.landings(0))
                dve.wait_ge(chunk_landed[gr.slot(c)], gr.landings(c))
                if c == 1:
                    nc.vector.tensor_tensor(sums[:, :], ring[:, gr.slot(0), :], ring[:, gr.slot(1), :],
                                            ALU.add).then_inc(chunk_summed, 2)
                else:
                    dve.wait_ge(chunk_summed, gr.first + c)
                    nc.vector.tensor_tensor(sums[:, :], sums[:, :], ring[:, gr.slot(c), :],
                                            ALU.add).then_inc(chunk_summed, 1)

            def add_pieces(gr):
                sums = part_deg[gr.parity]
                dve.wait_ge(chunk_summed, gr.first + gr.chunks - PIECED)
                for n, (what, width, piece, col) in enumerate(PIECE_PLAN):
                    if n:
                        dve.wait_ge(piece_step, n)
                    if what == "fold":
                        ins = nc.vector.tensor_tensor(sums[:, 0:width], sums[:, 0:width],
                                                      sums[:, width:2 * width], ALU.add)
                    elif what == "rows":
                        dve.wait_ge(deg_rows_made, gr.index + 1)
                        ins = nc.vector.scalar_tensor_tensor(out=sums[:, 0:width], in0=deg_rows_ps[:, 0:width],
                                                             scalar=1.0 / TW, in1=sums[:, 0:width],
                                                             op0=ALU.mult, op1=ALU.add)
                    else:
                        dve.wait_ge(piece_landed[piece], 16)
                        slot, col = gr.piece(col)
                        ins = nc.vector.tensor_tensor(sums[:, 0:width], sums[:, 0:width],
                                                      ring[:, slot, col:col + width], ALU.add)
                    ins.then_inc(piece_step, 1)

            def done(ins, gr, name):
                ins.then_inc(tail_step, 1)
                dve.wait_ge(tail_step, gr.step(name))

            def linear(gr):
                n = gr.blocks
                z_self, z_neigh = (z_ps[:, :, part, 0:gr.hb, :] for part in range(2))
                dve.wait_ge(deg_made, gr.index + 1)
                done(nc.vector.tensor_scalar(deg[:, 0:n], deg_ps[:, 0:n], 1.0, 1.0, ALU.add, ALU.max), gr, "DEG")
                done(nc.vector.reciprocal(inv_deg[:, 0:n], deg[:, 0:n]), gr, "INV_DEG")
                dve.wait_ge(z_made, gr.index + 1)
                done(nc.vector.tensor_tensor(by_half(z, gr), z_neigh, wide_by_half(inv_deg, gr), ALU.mult),
                     gr, "SCALED")
                done(nc.vector.tensor_tensor(by_half(z, gr), by_half(z, gr), z_self, ALU.add), gr, "Z")

            def residual(gr):
                n = gr.blocks
                zs, ys = z[:, 0:n, :], y[:, 0:n, :]
                if gr.last:
                    done(nc.vector.scalar_tensor_tensor(out=square[:, 0:n, :], in0=zs, scalar=0.0, in1=zs,
                                                        op0=ALU.max, op1=ALU.mult), gr, "SQUARE")
                    done(nc.vector.tensor_reduce(norm_sq[:, 0:n], square[:, 0:n, :], AX_X, ALU.add), gr, "NORM_SQ")
                dve.wait_ge(norm_made, gr.index + 1)
                done(nc.vector.tensor_scalar(norm[:, 0:n], norm[:, 0:n], L2_EPS, None, ALU.max), gr, "NORM_MAX")
                done(nc.vector.reciprocal(inv_norm[:, 0:n], norm[:, 0:n]), gr, "INV_NORM")
                dve.wait_ge(relu_made, gr.index + 1)
                done(nc.vector.tensor_tensor(ys, relu[:, 0:n, :], wide(inv_norm, gr), ALU.mult), gr, "UNIT")
                done(nc.vector.tensor_tensor(ys, ys, x_group[gr.parity][:, 0:n, :], ALU.add), gr, "Y")
                done(nc.vector.tensor_reduce(total[:, 0:n], ys, AX_X, ALU.add), gr, "SUM")
                if not gr.last:
                    done(nc.vector.tensor_scalar(neg_mean[:, 0:n], total[:, 0:n], -1.0 / D, None, ALU.mult),
                         gr, "NEG_MEAN")

            def layer_norm(gr):
                n = gr.blocks
                ys, sq = y[:, 0:n, :], square[:, 0:n, :]
                if gr.last:
                    done(nc.vector.scalar_tensor_tensor(out=ys, in0=wide(total, gr), scalar=-1.0 / D, in1=ys,
                                                        op0=ALU.mult, op1=ALU.add), gr, "CENTRED")
                    done(nc.vector.tensor_tensor(sq, ys, ys, ALU.mult), gr, "SQUARE2")
                    done(nc.vector.tensor_reduce(var[:, 0:n], sq, AX_X, ALU.add), gr, "VAR")
                dve.wait_ge(std_made, gr.index + 1)
                done(nc.vector.reciprocal(inv_std[:, 0:n], std[:, 0:n]), gr, "INV_STD")
                if not gr.last:
                    done(nc.vector.tensor_tensor(shift[:, 0:n], neg_mean[:, 0:n], inv_std[:, 0:n], ALU.mult),
                         gr, "SHIFT")
                else:
                    dve.wait_ge(out_free[gr.parity], gr.earlier * 16 + 16)
                    done(nc.vector.tensor_tensor(out_sb[gr.parity][:, 0:n, :], ys, wide(inv_std, gr), ALU.mult),
                         gr, "OUT")

            def body(gr, prev):
                for c in range(1, gr.chunks - (PIECED if gr.last else 0)):
                    add_chunk(gr, c)
                    for at, stage in ((gr.chunks // 4, linear), (3 * gr.chunks // 8, residual),
                                      (gr.chunks // 2, layer_norm)):
                        if prev and c == at:
                            stage(prev)

            each_group(dve, body)
            add_pieces(last_group)
            linear(last_group)
            residual(last_group)
            layer_norm(last_group)

        @block.tensor
        def _(pe):
            def multiply(gr, slot, at, width, j):
                for col in range(at, at + width, gr.cols):
                    for h in range(2):
                        half = slice(col + h * gr.half, col + (h + 1) * gr.half)
                        last = nc.tensor.matmul(hT_ps[gr.parity][h * D:(h + 1) * D, 0:gr.half], x_sb[:, j, :],
                                                ring[:, slot, half], start=(j == 0), stop=(j == NB - 1))
                    j += 1
                return last

            def transpose_x(gr):
                pe.wait_ge(x_group_staged, gr.index + 1)
                for k in range(gr.blocks):
                    rows, cols = gr.half_of(k)
                    last = nc.tensor.matmul(xT_ps[rows, cols], x_group[gr.parity][:, k, :], identity[:, :],
                                            start=True, stop=True)
                last.then_inc(xT_made, 1)

            def self_part(gr, prev):
                pe.wait_ge(xT_copied, gr.index + 1)
                if prev:
                    pe.wait_ge(tail_step, prev.step("Z"))
                for h in range(2):
                    nc.tensor.matmul(z_ps[:, h, 0, 0:gr.hb, :], ones[h * D:h * D + 1, :],
                                     bias_row[h * D:h * D + 1, 0:gr.hb, :], start=True, stop=False,
                                     skip_group_check=True)
                for k in range(gr.blocks):
                    rows, cols = gr.half_of(k)
                    for part, weight in ((0, w_self), (1, w_neigh)):
                        nc.tensor.matmul(z_ps[:, k // gr.hb, part, k % gr.hb, :], xT[rows, cols], weight[rows, :],
                                         start=False, stop=False, skip_group_check=True)

            def degree_rows(gr, src, width=CW, start=True, stop=True):
                blocks, step = width // gr.cols, min(gr.cols, BANK)
                for at in range(0, gr.cols, step):
                    for jj in range(blocks):
                        rows = slice(jj % TILES * TW, (jj % TILES + 1) * TW)
                        col = jj * gr.cols + at
                        last = nc.tensor.matmul(deg_rows_ps[rows, at:at + step], ones[:, 0:TW],
                                                src[:, col:col + step], start=(start and jj < TILES),
                                                stop=(stop and jj >= blocks - TILES))
                if stop:
                    last.then_inc(deg_rows_made, 1)

            def by_pieces(gr):
                for i, (at, width) in enumerate(zip(PIECE_AT, PIECES)):
                    pe.wait_ge(piece_landed[i], 16)
                    slot, col = gr.piece(at)
                    last = multiply(gr, slot, col, width, NB - (PIECED * CW - at) // gr.cols)
                    if i < TENSOR_SUMS:
                        degree_rows(gr, ring[:, slot, col:col + width], width,
                                    start=(i == 0), stop=(i == TENSOR_SUMS - 1))
                last.then_inc(chunk_multiplied, PIECED)

            def degrees(gr):
                pe.wait_ge(deg_rows_copied, gr.index + 1)
                for k in range(gr.blocks):
                    last = nc.tensor.matmul(deg_ps[:, k:k + 1], deg_rows[:, k * P:(k + 1) * P], copies[:, 0:1],
                                            start=True, stop=True)
                last.then_inc(deg_made, 1)

            def last_degrees(gr):
                pe.wait_ge(piece_step, len(PIECE_PLAN))
                for k in range(gr.blocks):
                    last = nc.tensor.matmul(deg_ps[:, k:k + 1], part_deg[gr.parity][:, k * P:(k + 1) * P],
                                            ones[:, 0:1], start=True, stop=True)
                last.then_inc(deg_made, 1)

            def neighbour_part(gr):
                pe.wait_ge(hT_copied, gr.index + 1)
                for k in range(gr.blocks):
                    rows, cols = gr.half_of(k)
                    last = nc.tensor.matmul(z_ps[:, k // gr.hb, 1, k % gr.hb, :], hT[rows, cols], w_neigh[rows, :],
                                            start=False, stop=(k % gr.hb == gr.hb - 1), skip_group_check=True)
                last.then_inc(z_made, 1)

            def body(gr, prev):
                for c in range(gr.chunks - (PIECED if gr.last else 0)):
                    if c == (gr.chunks // 2 if prev else 3 * gr.chunks // 4):
                        if not prev:
                            pe.wait_ge(weights_landed, 16 * WEIGHT_LOADS)
                        self_part(gr, prev)
                    if not prev and c % (CHUNKS // XPARTS) == 0:
                        pe.wait_ge(x_landed[c // (CHUNKS // XPARTS)], 16)
                    pe.wait_ge(chunk_landed[gr.slot(c)], gr.landings(c))
                    multiply(gr, gr.slot(c), 0, CW, c * gr.jb).then_inc(chunk_multiplied, 1)
                    if c == (gr.chunks // 8 if prev else gr.chunks // 2):
                        transpose_x(gr)
                        if prev:
                            pe.wait_ge(chunk_summed, prev.first + prev.chunks)
                            degree_rows(prev, part_deg[prev.parity])
                            neighbour_part(prev)
                            degrees(prev)

            pe.wait_ge(consts_set, 5)
            each_group(pe, body)
            by_pieces(last_group)
            last_degrees(last_group)
            neighbour_part(last_group)


def kernel(x, adj, L0_gnn_W, L0_gnn_b):
    import concourse.bacc as bacc
    from concourse.bass_utils import run_bass_kernel_spmd

    x, adj, w, b = (np.ascontiguousarray(a) for a in (x, adj, L0_gnn_W, L0_gnn_b))
    chunks = []
    for base, n in zip(BASE, GROUPS):
        jb = CW // (n * P)
        rows = adj.reshape(P, NB, N)[:, base:base + n].reshape(P, n, P, NB // jb, jb)
        chunks.append(rows.transpose(3, 2, 4, 1, 0).reshape(NB // jb, P, CW))
    arrays = {"x": x, "adj_chunks": np.concatenate(chunks), "w": w, "b": b}

    nc = bacc.Bacc("TRN2", target_bir_lowering=False, num_devices=1)
    args = [nc.dram_tensor(f"{n}_dram", a.shape, F32, kind="ExternalInput").ap() for n, a in arrays.items()]
    out = nc.dram_tensor("out_dram", (N, D), F32, kind="ExternalOutput").ap()
    gnn_resnorm(nc, *args, out)
    r = run_bass_kernel_spmd(nc, [{f"{n}_dram": a for n, a in arrays.items()}], core_ids=[0])
    return r.results[0]["out_dram"]
```
